# Optimizing a Trainium2 kernel written in Bass

```python
import numpy as np
import jax
import jax.numpy as jnp

def _softmax(x, axis=-1):
    return jax.nn.softmax(x, axis=axis)

def _gelu(x):
    return jax.nn.gelu(x, approximate=True)

def _silu(x):
    return jax.nn.silu(x)

def _sigmoid(x):
    return jax.nn.sigmoid(x)

def _layernorm(x, axis=-1, eps=1e-05):
    m = jnp.mean(x, axis=axis, keepdims=True)
    v = jnp.var(x, axis=axis, keepdims=True)
    return (x - m) / jnp.sqrt(v + eps)

def _scatter_add(tgt, idx, src, axis=0):
    return tgt.at[idx].add(src)

def _segment_sum(src, seg, n):
    return jax.ops.segment_sum(src, seg, n)
kernel_name = 'mk_adj_preln_d2_adj_r2_e87c9a'

def setup_inputs(seed: int=0):
    np.random.seed(seed)
    _w = jnp.asarray

    def _rec_inputs():
        import jax
        import jax.numpy as jnp
        _gk = jax.random.key(seed)
        x = -0.0001538 + 1 * jax.random.normal(jax.random.fold_in(_gk, 1), (64, 128, 384), jnp.float32)
        _w = (1.0 + jnp.arange(128, dtype=jnp.float32)) ** (-0.5)
        _w = _w / _w.mean()
        _pij = jnp.clip(0.015625 * _w[:, None] * _w[None, :], 0.0, 1.0)
        _a = jax.random.uniform(jax.random.fold_in(_gk, 2), (64, 128, 128)) < _pij
        _af = _a.astype(jnp.float32)
        adj = _af
        return (x, adj)
    x, adj = _rec_inputs()

    def _L0_gnn_setup():
        import jax, jax.numpy as jnp
        import numpy as np
        LN_EPS = 1e-12

        def _digcn_forward(hidden_state, adjacency_matrix, Wl, bl, Ws, bs, Wr, br, ln_w, ln_b):
            B, S, D = hidden_state.shape
            temper = jnp.asarray(D, jnp.float32) ** 0.5
            i = jnp.arange(S)
            upper = (i[None, :] > i[:, None]).astype(hidden_state.dtype)
            lower = (i[None, :] < i[:, None]).astype(hidden_state.dtype)

            def layer(h, params):
                wl, b_l, ws, b_s, wr, b_r, g, beta = params
                u = jnp.einsum('bid,bjd->bij', h, h) / temper
                a = jax.nn.softmax(u, axis=-1)
                delta = a * adjacency_matrix
                attn = delta / (jnp.sum(delta, axis=-1, keepdims=True) + 1e-10)
                hl = h @ wl.T + b_l
                hs = h @ ws.T + b_s
                hr = h @ wr.T + b_r
                diag_a = jnp.diagonal(attn, axis1=1, axis2=2)
                ctx = jnp.einsum('bij,bjd->bid', attn * upper, hl) + diag_a[..., None] * hs + jnp.einsum('bij,bjd->bid', attn * lower, hr)
                mean = ctx.mean(-1, keepdims=True)
                var = ctx.var(-1, keepdims=True)
                o = (ctx - mean) / jnp.sqrt(var + LN_EPS) * g + beta
                return (jax.nn.relu(o), None)
            out, _ = jax.lax.scan(layer, hidden_state, (Wl, bl, Ws, bs, Wr, br, ln_w, ln_b))
            return out
        key = jax.random.key(seed)
        ks = jax.random.split(key, 6)
        B, S, D, L = (8, 512, 384, 2)
        scale = (1.0 / D) ** 0.5
        hidden_state = jax.random.normal(ks[0], (B, S, D), jnp.float32)
        adjacency_matrix = (jax.random.uniform(ks[1], (B, S, S)) < 0.05).astype(jnp.float32)
        Wl = jax.random.normal(ks[2], (L, D, D), jnp.float32) * scale
        Ws = jax.random.normal(ks[3], (L, D, D), jnp.float32) * scale
        Wr = jax.random.normal(ks[4], (L, D, D), jnp.float32) * scale
        bl = jnp.zeros((L, D), jnp.float32)
        bs = jnp.zeros((L, D), jnp.float32)
        br = jnp.zeros((L, D), jnp.float32)
        ln_w = jnp.ones((L, D), jnp.float32)
        ln_b = jnp.zeros((L, D), jnp.float32)
        return dict(hidden_state=hidden_state, adjacency_matrix=adjacency_matrix, Wl=Wl, bl=bl, Ws=Ws, bs=bs, Wr=Wr, br=br, ln_w=ln_w, ln_b=ln_b)
    _L0_gnn_all = _L0_gnn_setup()
    _L0_gnn_in = {k: v for k, v in _L0_gnn_all.items() if k in ('Wl', 'bl', 'Ws', 'bs', 'Wr', 'br', 'ln_w', 'ln_b')}
    del _L0_gnn_all

    def _L1_gnn_setup():
        import jax, jax.numpy as jnp
        import numpy as np
        B, N, D, H = (8, 512, 384, 12)
        HD = D // H

        def _split_heads(x):
            b, n, _ = x.shape
            return x.reshape(b, n, H, HD).transpose(0, 2, 1, 3)
        key = jax.random.key(seed)
        ks = jax.random.split(key, 10)
        input_graph = jax.random.normal(ks[0], (B, N, D), dtype=jnp.float32)
        u = jax.random.uniform(ks[1], (B, N, N), dtype=jnp.float32)
        keep = jax.random.uniform(ks[2], (B, N, N)) < 0.15
        adj = jnp.where(keep, u, 0.0)
        s = 1.0 / np.sqrt(D)
        Wq = jax.random.normal(ks[3], (D, D), dtype=jnp.float32) * s
        bq = jnp.zeros((D,), dtype=jnp.float32)
        Wk = jax.random.normal(ks[4], (D, D), dtype=jnp.float32) * s
        bk = jnp.zeros((D,), dtype=jnp.float32)
        Wv = jax.random.normal(ks[5], (D, D), dtype=jnp.float32) * s
        bv = jnp.zeros((D,), dtype=jnp.float32)
        beta = jnp.asarray(0.1, dtype=jnp.float32)
        return {'input_graph': input_graph, 'adj': adj, 'Wq': Wq, 'bq': bq, 'Wk': Wk, 'bk': bk, 'Wv': Wv, 'bv': bv, 'beta': beta}
    _L1_gnn_all = _L1_gnn_setup()
    _L1_gnn_in = {k: v for k, v in _L1_gnn_all.items() if k in ('Wq', 'bq', 'Wk', 'bk', 'Wv', 'bv', 'beta')}
    del _L1_gnn_all
    return {'x': x, 'adj': adj, 'L0_gnn_Wl': _L0_gnn_in['Wl'], 'L0_gnn_bl': _L0_gnn_in['bl'], 'L0_gnn_Ws': _L0_gnn_in['Ws'], 'L0_gnn_bs': _L0_gnn_in['bs'], 'L0_gnn_Wr': _L0_gnn_in['Wr'], 'L0_gnn_br': _L0_gnn_in['br'], 'L0_gnn_ln_w': _L0_gnn_in['ln_w'], 'L0_gnn_ln_b': _L0_gnn_in['ln_b'], 'L1_gnn_Wq': _L1_gnn_in['Wq'], 'L1_gnn_bq': _L1_gnn_in['bq'], 'L1_gnn_Wk': _L1_gnn_in['Wk'], 'L1_gnn_bk': _L1_gnn_in['bk'], 'L1_gnn_Wv': _L1_gnn_in['Wv'], 'L1_gnn_bv': _L1_gnn_in['bv'], 'L1_gnn_beta': _L1_gnn_in['beta']}

def reference(x, adj, L0_gnn_Wl, L0_gnn_bl, L0_gnn_Ws, L0_gnn_bs, L0_gnn_Wr, L0_gnn_br, L0_gnn_ln_w, L0_gnn_ln_b, L1_gnn_Wq, L1_gnn_bq, L1_gnn_Wk, L1_gnn_bk, L1_gnn_Wv, L1_gnn_bv, L1_gnn_beta):
    import jax
    import jax.numpy as jnp

    def _L0_gnn_ref(hidden_state, adjacency_matrix, Wl, bl, Ws, bs, Wr, br, ln_w, ln_b):
        import jax, jax.numpy as jnp
        import numpy as np
        LN_EPS = 1e-12

        def _digcn_forward(hidden_state, adjacency_matrix, Wl, bl, Ws, bs, Wr, br, ln_w, ln_b):
            B, S, D = hidden_state.shape
            temper = jnp.asarray(D, jnp.float32) ** 0.5
            i = jnp.arange(S)
            upper = (i[None, :] > i[:, None]).astype(hidden_state.dtype)
            lower = (i[None, :] < i[:, None]).astype(hidden_state.dtype)

            def layer(h, params):
                wl, b_l, ws, b_s, wr, b_r, g, beta = params
                u = jnp.einsum('bid,bjd->bij', h, h) / temper
                a = jax.nn.softmax(u, axis=-1)
                delta = a * adjacency_matrix
                attn = delta / (jnp.sum(delta, axis=-1, keepdims=True) + 1e-10)
                hl = h @ wl.T + b_l
                hs = h @ ws.T + b_s
                hr = h @ wr.T + b_r
                diag_a = jnp.diagonal(attn, axis1=1, axis2=2)
                ctx = jnp.einsum('bij,bjd->bid', attn * upper, hl) + diag_a[..., None] * hs + jnp.einsum('bij,bjd->bid', attn * lower, hr)
                mean = ctx.mean(-1, keepdims=True)
                var = ctx.var(-1, keepdims=True)
                o = (ctx - mean) / jnp.sqrt(var + LN_EPS) * g + beta
                return (jax.nn.relu(o), None)
            out, _ = jax.lax.scan(layer, hidden_state, (Wl, bl, Ws, bs, Wr, br, ln_w, ln_b))
            return out
        return _digcn_forward(hidden_state, adjacency_matrix, Wl, bl, Ws, bs, Wr, br, ln_w, ln_b)

    def _L1_gnn_ref(input_graph, adj, Wq, bq, Wk, bk, Wv, bv, beta):
        import jax, jax.numpy as jnp
        import numpy as np
        B, N, D, H = (8, 512, 384, 12)
        HD = D // H

        def _split_heads(x):
            b, n, _ = x.shape
            return x.reshape(b, n, H, HD).transpose(0, 2, 1, 3)
        q = _split_heads(input_graph @ Wq + bq)
        k = _split_heads(input_graph @ Wk + bk)
        v = _split_heads(input_graph @ Wv + bv)
        scores = jnp.einsum('bhqd,bhkd->bhqk', q, k) / jnp.sqrt(jnp.asarray(HD, input_graph.dtype))
        adj_e = adj[:, None, :, :]
        scores = scores + beta * adj_e
        scores = jnp.where(adj_e > 0, scores, jnp.asarray(-9000000000000000.0, scores.dtype))
        probs = jax.nn.softmax(scores, axis=-1)
        out = jnp.einsum('bhqk,bhkd->bhqd', probs, v)
        return out.transpose(0, 2, 1, 3).reshape(input_graph.shape[0], input_graph.shape[1], D)
    h = jnp.maximum(_layernorm(x, axis=-1), 0.0)
    x = x + _L0_gnn_ref(h, adj, L0_gnn_Wl, L0_gnn_bl, L0_gnn_Ws, L0_gnn_bs, L0_gnn_Wr, L0_gnn_br, L0_gnn_ln_w, L0_gnn_ln_b)
    h = jnp.maximum(_layernorm(x, axis=-1), 0.0)
    x = x + _L1_gnn_ref(h, adj, L1_gnn_Wq, L1_gnn_bq, L1_gnn_Wk, L1_gnn_bk, L1_gnn_Wv, L1_gnn_bv, L1_gnn_beta)
    return x

_drawn_inputs = setup_inputs


def setup_inputs(seed=0):
    import zlib

    import numpy as np

    out = dict(_drawn_inputs(seed))
    spreads = {'L0_gnn_bl': (0.0, 0.1),
     'L0_gnn_bs': (0.0, 0.316),
     'L0_gnn_br': (0.0, 0.1),
     'L0_gnn_ln_w': (1.0, 0.2),
     'L0_gnn_ln_b': (0.0, 0.1),
     'L1_gnn_bq': (0.0, 0.8),
     'L1_gnn_bk': (0.0, 0.8),
     'L1_gnn_bv': (0.0, 0.1)}
    factors = {}
    for name, (base, spread) in spreads.items():
        noise = np.random.default_rng([zlib.crc32(name.encode()), seed]).standard_normal(out[name].shape)
        drawn = base * np.exp(spread * noise) if base else spread * noise
        out[name] = jnp.asarray(drawn.astype(out[name].dtype))
    for name, factor in factors.items():
        out[name] = (out[name] * factor).astype(out[name].dtype)
    return out
```

```python
import numpy as np

import concourse.bass as bass
from concourse import mybir
from concourse.alu_op_type import AluOpType as ALU

F32 = mybir.dt.float32
F16 = mybir.dt.float16
ACT = mybir.ActivationFunctionType
X_AXIS = mybir.AxisListType.X

ITEMS, S, D = 64, 128, 384
KT = D // 128
HEADS, HD = 12, 32
ROWS = 128 // HD
LN_EPS = 1e-5
CTX_EPS, SUM_EPS = 1e-12, 1e-10
U_SCALE = float(np.float32(1.0) / np.sqrt(np.float32(D)))
W_SCALE = 64.0
A_SCALE = float(np.float32(1.0) / np.sqrt(np.float32(HD)) / np.float32(W_SCALE ** 2))
MASKED = -(2.0 ** 80)
LEFT, SELF, RIGHT = range(3)
QW, KW, VW = 6, 7, 8
HI, LO = 0, 1


def graph_block_program(nc: bass.Bass, x, adj, wl, bl, ws, bs, wr, br, ln_w, ln_b,
                        wq, bq, wk, bk, wv, bv, beta, out):

    def sb(name, shape, dt=F32):
        return nc.alloc_sbuf_tensor(name, shape, dt)

    def sem(name, n=None):
        return nc.alloc_semaphore(name) if n is None else [nc.alloc_semaphore(f"{name}{i}") for i in range(n)]

    w_raw = sb("w_raw", [128, 9, KT, D])
    w_part = [sb("w_hi", [128, 9, KT, D], F16), sb("w_lo", [128, 9, KT, D], F16)]
    bias3 = sb("bias3", [128, 2, 3, D])
    gain, shift = sb("gain", [128, 2, D]), sb("shift", [128, 2, D])
    bv_rows = sb("bv_rows", [128, D])
    bqk = sb("bqk", [128, 2, KT])
    beta_col = sb("beta_col", [128, 1])
    beta_scaled = sb("beta_scaled", [128, 1])
    ident = sb("ident", [128, 128])
    tri = sb("tri", [128, 2, 128])
    neg_half = sb("neg_half", [128, 1])

    x_in = [sb("x_in0", [128, D]), sb("x_in1", [128, D])]
    adj_in = [sb(f"adj_in{i}", [128, S]) for i in range(3)]
    h_rows = [sb("h_rows0", [128, D]), None, sb("h_rows2", [128, D])]
    hT = [[sb(f"hT{i}_hi", [128, KT, S], F16), sb(f"hT{i}_lo", [128, KT, S], F16)] for i in range(3)]
    u_max, u_nbias = [sb(f"u_max{i}", [128, 1]) for i in range(2)], [sb(f"u_nbias{i}", [128, 1]) for i in range(2)]
    e_rows = [sb(f"e_rows{i}", [128, S]) for i in range(2)]
    e_sum = [sb(f"e_sum{i}", [128, 1]) for i in range(2)]
    delta = [sb(f"delta{i}", [128, S]) for i in range(2)]
    delta_sum = [sb(f"delta_sum{i}", [128, 1]) for i in range(2)]
    diag = [sb(f"diag{i}", [128, 1]) for i in range(2)]
    diag_junk = [sb(f"diag_junk{i}", [128, S]) for i in range(2)]
    deltaT = [sb(f"deltaT{i}", [128, 2, S]) for i in range(2)]
    proj = [sb(f"proj{i}", [128, 3, D]) for i in range(2)]
    ctx = [sb(f"ctx{i}", [128, D]) for i in range(2)]
    den = [sb(f"den{i}", [128, 2]) for i in range(2)]
    o_rows = sb("o_rows", [128, D])
    scaled = [sb("scaled0", [128, D]), sb("scaled1", [128, D])]
    y_rows = sb("y_rows", [128, D])
    x_mid = sb("x_mid", [128, D])
    stats = [sb(f"stats{i}", [128, 6]) for i in range(4)]
    mean_var = [sb(f"mean_var{i}", [128, 2]) for i in range(4)]
    var_eps = [sb(f"var_eps{i}", [128, 1]) for i in range(4)]
    rstd = [sb(f"rstd{i}", [128, 1]) for i in range(4)]

    qT = [sb("qT_hi", [128, KT, S], F16), sb("qT_lo", [128, KT, S], F16)]
    kT = [sb("kT_hi", [128, KT, S], F16), sb("kT_lo", [128, KT, S], F16)]
    v_rows = sb("v_rows", [128, D])
    adj_cut, adj_beta, adj_bias = sb("adj_cut", [128, S]), sb("adj_beta", [128, S]), sb("adj_bias", [128, S])
    scores = sb("scores", [128, ROWS, KT, S])
    s_max, s_nbias = sb("s_max", [128, ROWS, KT]), sb("s_nbias", [128, ROWS, KT])
    probs = sb("probs", [128, ROWS, KT, S])
    p_sum, p_recip = sb("p_sum", [128, KT, ROWS]), sb("p_recip", [128, KT, ROWS])
    probsT = sb("probsT", [128, ROWS, KT, S])
    oT = sb("oT", [128, KT, S])
    x_bv = sb("x_bv", [128, D])
    att = sb("att", [128, D])
    y_out = sb("y_out", [128, D])

    b_tr, b_u, b_c, b_d, b_e, b_ctx, b_g, b_h = [
        nc.alloc_psum_tensor(f"bank_{n}", [128, 512], F32) for n in ("tr", "u", "c", "d", "e", "ctx", "g", "h")]
    b_proj = [b_c, b_e, b_d]
    b_score = [b_d, b_e, b_g, b_h]
    b_pT = [b_g, b_h, b_g, b_h]

    def tiles(bank):
        return bank[:, 0:D].rearrange("p (t n) -> p t n", t=KT)

    w_loaded, w_hi_made, w_lo_made = sem("w_loaded", 9), sem("w_hi_made"), sem("w_lo_made")
    consts_loaded, consts_made = sem("consts_loaded"), sem("consts_made")
    fills_made, scaled_consts_made = sem("fills_made"), sem("scaled_consts_made")
    x_loaded, adj_loaded = sem("x_loaded", 2), sem("adj_loaded", 3)
    out_stored = sem("out_stored")
    stats_made, moments_made = sem("stats_made", 4), sem("moments_made", 4)
    veps_made, rstd_made = sem("veps_made", 4), sem("rstd_made", 4)
    h_made = {0: sem("h_made0"), 2: sem("h_made2")}
    tr_done = sem("tr_done", 3)
    hT_hi_made, hT_lo_made = sem("hT_hi_made", 3), sem("hT_lo_made", 3)
    u_done, u_max_made, u_nbias_made = sem("u_done", 2), sem("u_max_made", 2), sem("u_nbias_made", 2)
    e_made, delta_made, diag_made = sem("e_made", 2), sem("delta_made", 2), sem("diag_made", 2)
    dT_done, dT_made = sem("dT_done", 2), sem("dT_made", 2)
    proj_done = [sem(f"proj_done{i}_", 3) for i in range(2)]
    proj_copied = [sem(f"proj_copied{i}_", 3) for i in range(2)]
    proj_biased = [sem(f"proj_biased{i}_", 3) for i in range(2)]
    ctx_done, ctx_made = sem("ctx_done", 2), sem("ctx_made", 2)
    den_made, den_sq_made = sem("den_made", 2), sem("den_sq_made", 2)
    scaled_made, o_made, y_made = sem("scaled_made", 2), sem("o_made"), sem("y_made")
    x_mid_made, x_bv_made = sem("x_mid_made"), sem("x_bv_made")
    q_done, k_done, v_done = sem("q_done"), sem("k_done"), sem("v_done")
    q_hi_made, k_hi_made = sem("q_hi_made"), sem("k_hi_made")
    q_made, k_made, v_made = sem("q_made"), sem("k_made"), sem("v_made")
    cut_made, adj_beta_made, adj_bias_made = sem("cut_made"), sem("adj_beta_made"), sem("adj_bias_made")
    s_done, s_made, s_nbias_made = sem("s_done", ROWS), sem("s_made", ROWS), sem("s_nbias_made", ROWS)
    p_made, pT_done, pT_made = sem("p_made", ROWS), sem("pT_done", ROWS), sem("pT_made", ROWS)
    pv_done, oT_made, o_done = sem("pv_done"), sem("oT_made"), sem("o_done")
    recip_made, att_made, y_out_made = sem("recip_made"), sem("att_made"), sem("y_out_made")

    def counts(eng, t):
        if isinstance(t, int):
            return [min(max(t + 1 - k, 0), ITEMS) for k in range(4)]
        return [eng.to_reg(t + 1), t, eng.to_reg(t - 1), eng.to_reg(t - 2)]

    def dma_counts(eng, t):
        if isinstance(t, int):
            return [16 * n for n in counts(eng, t)]
        return [eng.to_reg((t + 1) * 16), eng.to_reg(t * 16), eng.to_reg((t - 1) * 16), eng.to_reg((t - 2) * 16)]

    def run_steps(eng, step, between=None):
        for t in range(3):
            step(t, counts(eng, t), (True, t >= 1, t >= 2))
            if between is not None and t == 0:
                between()
        with eng.Fori(3, ITEMS) as t:
            step(t, counts(eng, t), (True, True, True))
        for t in range(ITEMS, ITEMS + 2):
            step(t, counts(eng, t), (False, t == ITEMS, True))

    block = nc.Block()
    block.__enter__()

    @block.sync
    def _(sp):
        w_src = [wl[0], ws[0], wr[0], wl[1], ws[1], wr[1], wq, wk, wv]

        def load_weight(n):
            sp.dma_start(w_raw[:, n], w_src[n].rearrange("(k p) n -> p k n", p=128)).then_inc(w_loaded[n], 16)

        def step(t, c, on):
            if on[0]:
                sp.wait_ge(h_made[0], c[1])
                sp.dma_start(x_in[0][:, :], x[bass.ds(t, 1)].rearrange("o s d -> (o s) d")).then_inc(x_loaded[0], 16)
                sp.wait_ge(delta_made[0], c[1])
                sp.dma_start(adj_in[0][:, :], adj[bass.ds(t, 1)].rearrange("o s d -> (o s) d")).then_inc(adj_loaded[0], 16)
            if isinstance(t, int) and t == 0:
                for n in (LEFT, RIGHT, SELF):
                    load_weight(n)
                load_constants()
                for n in range(3, 9):
                    load_weight(n)
            if on[1]:
                sp.wait_ge(delta_made[1], c[2])
                sp.dma_start(adj_in[1][:, :], adj[bass.ds(t - 1, 1)].rearrange("o s d -> (o s) d")).then_inc(adj_loaded[1], 16)
                sp.wait_ge(x_mid_made, c[2])
                sp.dma_start(x_in[1][:, :], x[bass.ds(t - 1, 1)].rearrange("o s d -> (o s) d")).then_inc(x_loaded[1], 16)
                sp.wait_ge(cut_made, c[2])
                sp.wait_ge(adj_beta_made, c[2])
                sp.dma_start(adj_in[2][:, :], adj[bass.ds(t - 1, 1)].rearrange("o s d -> (o s) d")).then_inc(adj_loaded[2], 16)
            if on[2]:
                sp.wait_ge(y_out_made, c[2])
                sp.dma_start(out[bass.ds(t - 2, 1)].rearrange("o s d -> (o s) d"), y_out[:, :]).then_inc(out_stored, 16)

        def load_constants():
            for l in range(2):
                for m, b in ((LEFT, bl), (SELF, bs), (RIGHT, br)):
                    sp.dma_start(bias3[:, l, m, :], row(b, l)).then_inc(consts_loaded, 16)
            for dst, src in ((gain, ln_w), (shift, ln_b)):
                for l in range(2):
                    sp.dma_start(dst[:, l, :], row(src, l)).then_inc(consts_loaded, 16)
            sp.dma_start(bv_rows[:, :], bv.rearrange("(o n) -> o n", o=1).broadcast_to([128, D])).then_inc(consts_loaded, 16)
            with nc.allow_non_contiguous_dma(reason="two small bias columns"):
                sp.dma_start(bqk[:, 0, :], bq.rearrange("(t p) -> p t", p=128)).then_inc(consts_loaded, 16)
                sp.dma_start(bqk[:, 1, :], bk.rearrange("(t p) -> p t", p=128)).then_inc(consts_loaded, 16)
            sp.dma_start(beta_col[:, :], beta.broadcast_to([128, 1])).then_inc(consts_loaded, 16)

        def row(a, l):
            return a[l:l + 1, :].broadcast_to([128, D])

        run_steps(sp, step)
        sp.wait_ge(out_stored, 16 * ITEMS)

    N_CONSTS = 14

    @block.tensor
    def _(pe):
        def transpose_rows(src, last_sem):
            for k in range(KT):
                last = nc.tensor.transpose(b_tr[:, k * S:(k + 1) * S], src[:, k * 128:(k + 1) * 128], ident[:, :])
            last.then_inc(last_sem, 1)

        def project_rows(bank, i, n, done):
            for k in range(KT):
                for a, b in ((HI, HI), (HI, LO), (LO, HI)):
                    last = nc.tensor.matmul(bank[:, 0:D], hT[i][a][:, k, :], w_part[b][:, n, k, :],
                                            start=(k == 0 and (a, b) == (HI, HI)),
                                            stop=(k == KT - 1 and (a, b) == (LO, HI)))
            last.then_inc(done, 1)

        def project_columns(bank, i, n, done):
            for m in range(KT):
                for k in range(KT):
                    for a, b in ((HI, HI), (HI, LO), (LO, HI)):
                        last = nc.tensor.matmul(bank[:, m * S:(m + 1) * S],
                                                w_part[a][:, n, k, m * 128:(m + 1) * 128], hT[i][b][:, k, :],
                                                start=(k == 0 and (a, b) == (HI, HI)),
                                                stop=(k == KT - 1 and (a, b) == (LO, HI)))
            last.then_inc(done, 1)

        def similarity(i):
            for k in range(KT):
                for a, b in ((HI, HI), (HI, LO), (LO, HI)):
                    last = nc.tensor.matmul(b_u[:, 0:S], hT[i][a][:, k, :], hT[i][b][:, k, :],
                                            start=(k == 0 and (a, b) == (HI, HI)),
                                            stop=(k == KT - 1 and (a, b) == (LO, HI)))
            last.then_inc(u_done[i], 1)

        def transpose_delta(i):
            nc.tensor.transpose(b_u[:, S:2 * S], delta[i][:, :], ident[:, :]).then_inc(dT_done[i], 1)

        def context(i):
            nc.tensor.matmul(b_ctx[:, 0:D], deltaT[i][:, 0, :], proj[i][:, LEFT, :], start=True, stop=False)
            nc.tensor.matmul(b_ctx[:, 0:D], deltaT[i][:, 1, :], proj[i][:, RIGHT, :], start=False,
                             stop=True).then_inc(ctx_done[i], 1)

        def transpose_probs(r):
            for k in range(KT):
                last = nc.tensor.transpose(b_pT[r][:, k * S:(k + 1) * S], probs[:, r, k, :], ident[:, :])
            last.then_inc(pT_done[r], 1)

        def scores_of(k, quads):
            for a, b in ((HI, HI), (HI, LO), (LO, HI)):
                for r in quads:
                    quad = slice(r * HD, (r + 1) * HD)
                    last = nc.tensor.matmul(b_score[r][:, k * S:(k + 1) * S], qT[a][quad, k, :], kT[b][quad, k, :],
                                            start=((a, b) == (HI, HI)), stop=((a, b) == (LO, HI)))
                    if k == KT - 1 and (a, b) == (LO, HI):
                        last.then_inc(s_done[r], 1)

        def step(t, c, on):
            if on[2]:
                pe.wait_ge(w_lo_made, 9)
                pe.wait_ge(hT_lo_made[2], c[2])
                pe.wait_ge(proj_copied[0][SELF], c[1])
                project_rows(b_e, 2, VW, v_done)
            if on[1]:
                pe.wait_ge(o_made, c[1])
                pe.wait_ge(hT_lo_made[2], c[2])
                transpose_rows(o_rows, tr_done[1])
            if on[2]:
                pe.wait_ge(q_made, c[2])
                pe.wait_ge(k_made, c[2])
                pe.wait_ge(oT_made, c[3])
                pe.wait_ge(att_made, c[3])
                scores_of(0, (0, 2, 3))
                pe.wait_ge(v_made, c[2])
                scores_of(0, (1,))
                scores_of(1, (0, 2, 3, 1))
                scores_of(2, (0, 2, 3, 1))
            if on[1]:
                pe.wait_ge(w_lo_made, 6)
                pe.wait_ge(hT_lo_made[1], c[1])
                pe.wait_ge(dT_made[0], c[1])
                similarity(1)
                pe.wait_ge(q_made, c[2])
                project_rows(b_c, 1, 3 + LEFT, proj_done[1][LEFT])
                pe.wait_ge(k_made, c[2])
                pe.wait_ge(s_made[0], c[2])
                project_rows(b_d, 1, 3 + RIGHT, proj_done[1][RIGHT])
                pe.wait_ge(delta_made[1], c[1])
                transpose_delta(1)
                pe.wait_ge(s_made[1], c[2])
                pe.wait_ge(proj_copied[0][SELF], c[1])
                project_rows(b_e, 1, 3 + SELF, proj_done[1][SELF])
            if on[0]:
                pe.wait_ge(h_made[0], c[0])
                pe.wait_ge(hT_lo_made[1], c[1])
                transpose_rows(h_rows[0], tr_done[0])
            if on[1]:
                pe.wait_ge(dT_made[1], c[1])
                pe.wait_ge(proj_biased[1][LEFT], c[1])
                pe.wait_ge(proj_biased[1][RIGHT], c[1])
                pe.wait_ge(ctx_made[0], c[1])
                context(1)
            if on[2]:
                pe.wait_ge(p_made[0], c[2])
                pe.wait_ge(s_made[2], c[2])
                transpose_probs(0)
                pe.wait_ge(p_made[1], c[2])
                pe.wait_ge(s_made[3], c[2])
                transpose_probs(1)
            if on[0]:
                pe.wait_ge(w_lo_made, 3)
                pe.wait_ge(hT_lo_made[0], c[0])
                pe.wait_ge(dT_made[1], c[1])
                similarity(0)
            if on[0]:
                pe.wait_ge(proj_copied[1][LEFT], c[1])
                project_rows(b_c, 0, LEFT, proj_done[0][LEFT])
            if on[2]:
                pe.wait_ge(p_made[2], c[2])
                pe.wait_ge(pT_made[0], c[2])
                transpose_probs(2)
            if on[2]:
                pe.wait_ge(p_made[3], c[2])
                pe.wait_ge(pT_made[1], c[2])
                transpose_probs(3)
            if on[0]:
                pe.wait_ge(proj_biased[1][RIGHT], c[1])
                project_rows(b_d, 0, RIGHT, proj_done[0][RIGHT])
            if on[2]:
                pe.wait_ge(v_made, c[2])
                for r in range(ROWS):
                    pe.wait_ge(pT_made[r], c[2])
                for k in range(KT):
                    for r in range(ROWS):
                        h = k * ROWS + r
                        last = nc.tensor.matmul(b_g[r * HD:(r + 1) * HD, k * S:(k + 1) * S],
                                                v_rows[:, h * HD:(h + 1) * HD], probsT[:, r, k, :],
                                                start=True, stop=True)
                last.then_inc(pv_done, 1)
            if on[0]:
                pe.wait_ge(delta_made[0], c[0])
                transpose_delta(0)
                pe.wait_ge(proj_biased[1][SELF], c[1])
                project_rows(b_e, 0, SELF, proj_done[0][SELF])
            if on[1]:
                pe.wait_ge(h_made[2], c[1])
                pe.wait_ge(hT_lo_made[0], c[0])
                transpose_rows(h_rows[2], tr_done[2])
            if on[2]:
                pe.wait_ge(oT_made, c[2])
                for k in range(KT):
                    last = nc.tensor.transpose(b_h[:, k * 128:(k + 1) * 128], oT[:, k, :], ident[:, :])
                last.then_inc(o_done, 1)
            if on[0]:
                pe.wait_ge(dT_made[0], c[0])
                pe.wait_ge(proj_biased[0][LEFT], c[0])
                pe.wait_ge(proj_biased[0][RIGHT], c[0])
                pe.wait_ge(ctx_made[1], c[1])
                context(0)
            if on[1]:
                pe.wait_ge(w_lo_made, 9)
                pe.wait_ge(hT_lo_made[2], c[1])
                pe.wait_ge(proj_copied[0][LEFT], c[0])
                project_columns(b_c, 2, QW, q_done)
                pe.wait_ge(proj_biased[0][RIGHT], c[0])
                project_columns(b_d, 2, KW, k_done)

        pe.wait_ge(fills_made, 3)
        run_steps(pe, step)

    @block.scalar
    def _(act):
        def split_weights(names):
            for n in names:
                act.wait_ge(w_loaded[n], 16)
                nc.scalar.activation(w_part[HI][:, n], w_raw[:, n], ACT.Copy, scale=W_SCALE).then_inc(w_hi_made, 1)

        def high_part(i, now):
            act.wait_ge(tr_done[i], now)
            nc.scalar.activation(hT[i][HI][:, :, :], tiles(b_tr), ACT.Relu).then_inc(hT_hi_made[i], 1)

        def exp_u(i, now):
            act.wait_ge(u_nbias_made[i], now)
            nc.scalar.activation(e_rows[i][:, :], b_u[:, 0:S], ACT.Exp, bias=u_nbias[i][:, :], scale=U_SCALE,
                                 accum_out=e_sum[i][:, :]).then_inc(e_made[i], 1)

        def copy_proj(i, m, now):
            act.wait_ge(proj_done[i][m], now)
            nc.scalar.activation(proj[i][:, m, :], b_proj[m][:, 0:D], ACT.Copy).then_inc(proj_copied[i][m], 1)

        def exp_scores(r, now, before):
            act.wait_ge(s_nbias_made[r], now)
            act.wait_ge(pT_done[r], before)
            for k in range(KT):
                last = nc.scalar.activation(probs[:, r, k, :], scores[:, r, k, :], ACT.Exp,
                                            bias=s_nbias[:, r, k:k + 1], scale=A_SCALE,
                                            accum_out=p_sum[:, k, r:r + 1])
            last.then_inc(p_made[r], 1)

        def copy_pT(r, now, before):
            act.wait_ge(pT_done[r], now)
            act.wait_ge(pv_done, before)
            nc.scalar.activation(probsT[:, r, :, :], tiles(b_pT[r]), ACT.Copy).then_inc(pT_made[r], 1)

        def step(t, c, on):
            if on[2]:
                act.wait_ge(v_done, c[2])
                act.wait_ge(pv_done, c[3])
                nc.scalar.activation(v_rows[:, :], b_e[:, 0:D], ACT.Copy, scale=1.0 / W_SCALE).then_inc(v_made, 1)
            if on[1]:
                act.wait_ge(proj_done[1][SELF], c[2])
                high_part(1, c[1])
                act.wait_ge(delta_made[1], c[2])
                act.wait_ge(den_made[1], c[2])
                exp_u(1, c[1])
            if on[2]:
                act.wait_ge(recip_made, c[3])
                exp_scores(0, c[2], c[3])
            if on[1]:
                act.wait_ge(ctx_done[1], c[2])
                copy_proj(1, LEFT, c[1])
            if on[2]:
                exp_scores(1, c[2], c[3])
            if on[2]:
                exp_scores(2, c[2], c[3])
            if on[0]:
                act.wait_ge(proj_done[0][SELF], c[1])
                high_part(0, c[0])
            if on[2]:
                exp_scores(3, c[2], c[3])
                copy_pT(0, c[2], c[3])
                copy_pT(1, c[2], c[3])
            if on[0]:
                act.wait_ge(delta_made[0], c[1])
                act.wait_ge(den_made[0], c[1])
                exp_u(0, c[0])
            if on[0]:
                act.wait_ge(ctx_done[0], c[1])
                copy_proj(0, LEFT, c[0])
            if on[2]:
                copy_pT(2, c[2], c[3])
                copy_pT(3, c[2], c[3])
            if on[2]:
                act.wait_ge(pv_done, c[2])
                act.wait_ge(o_done, c[3])
                nc.scalar.activation(oT[:, :, :], tiles(b_g), ACT.Copy).then_inc(oT_made, 1)
            if on[0]:
                act.wait_ge(ctx_made[0], c[1])
                copy_proj(0, SELF, c[0])
            if on[1]:
                act.wait_ge(v_done, c[2])
                high_part(2, c[1])
                for dst, bank, j, done, made in ((qT, b_c, 0, q_done, q_hi_made), (kT, b_d, 1, k_done, k_hi_made)):
                    act.wait_ge(done, c[1])
                    act.wait_ge(s_done[1], c[2])
                    for m in range(KT):
                        last = nc.scalar.activation(dst[HI][:, m, :], bank[:, m * S:(m + 1) * S], ACT.Identity,
                                                    bias=bqk[:, j, m:m + 1])
                    last.then_inc(made, 1)

        split_weights((LEFT, RIGHT, SELF))
        act.wait_ge(scaled_consts_made, 3)
        run_steps(act, step, between=lambda: split_weights(range(3, 9)))

    @block.vector
    def _(dve):
        def split_weights(names):
            for n in names:
                dve.wait_ge(w_hi_made, {LEFT: 1, RIGHT: 2, SELF: 3}.get(n, n + 1))
                nc.vector.scalar_tensor_tensor(w_part[LO][:, n], w_raw[:, n], W_SCALE, w_part[HI][:, n],
                                               ALU.mult, ALU.subtract).then_inc(w_lo_made, 1)

        def moments(j, src, now):
            nc.vector.bn_stats(stats[j][:, :], src[:, :]).then_inc(stats_made[j], 1)
            dve.wait_ge(fills_made, 3)
            dve.wait_ge(stats_made[j], now)
            nc.vector.bn_aggr(mean_var[j][:, :], stats[j][:, :]).then_inc(moments_made[j], 1)

        def low_part(i, now):
            dve.wait_ge(hT_hi_made[i], now)
            nc.vector.scalar_tensor_tensor(hT[i][LO][:, :, :], tiles(b_tr), 0.0, hT[i][HI][:, :, :],
                                           ALU.max, ALU.subtract).then_inc(hT_lo_made[i], 1)

        def max_u(i, now):
            dve.wait_ge(u_done[i], now)
            nc.vector.reduce_max(u_max[i][:, :], b_u[:, 0:S], X_AXIS).then_inc(u_max_made[i], 1)
            dve.wait_ge(u_max_made[i], now)
            nc.vector.tensor_scalar(u_nbias[i][:, :], u_max[i][:, :], -U_SCALE, None,
                                    ALU.mult).then_inc(u_nbias_made[i], 1)

        def mask_delta(i, now, before, dma_now):
            dve.wait_ge(e_made[i], now)
            dve.wait_ge(adj_loaded[i], dma_now)
            dve.wait_ge(dT_done[i], before)
            dve.wait_ge(den_made[i], before)
            nc.vector.tensor_tensor_reduce(out=delta[i][:, :], in0=e_rows[i][:, :], in1=adj_in[i][:, :], scale=1.0,
                                           scalar=0.0, op0=ALU.mult, op1=ALU.add,
                                           accum_out=delta_sum[i][:, :]).then_inc(delta_made[i], 1)

        def take_diag(i, now):
            dve.wait_ge(delta_made[i], now)
            nc.vector.tensor_tensor_reduce(out=diag_junk[i][:, :], in0=delta[i][:, :], in1=ident[:, :], scale=1.0,
                                           scalar=0.0, op0=ALU.mult, op1=ALU.add,
                                           accum_out=diag[i][:, :]).then_inc(diag_made[i], 1)

        def mask_deltaT(i, now, before):
            dve.wait_ge(dT_done[i], now)
            dve.wait_ge(ctx_done[i], before)
            both = b_u[:, S:2 * S].rearrange("p (o n) -> p o n", o=1).broadcast_to([128, 2, S])
            nc.vector.tensor_tensor(deltaT[i][:, :, :], both, tri[:, :, :], ALU.mult).then_inc(dT_made[i], 1)

        def bias_proj(i, m, now, used, before):
            dve.wait_ge(proj_done[i][m], now)
            dve.wait_ge(used[i], before)
            nc.vector.tensor_tensor(proj[i][:, m, :], b_proj[m][:, 0:D], bias3[:, i, m, :],
                                    ALU.add).then_inc(proj_biased[i][m], 1)

        def low_columns(dst, bank, j, hi_made, made, now):
            dve.wait_ge(hi_made, now)
            for m in range(KT):
                last = nc.vector.scalar_tensor_tensor(dst[LO][:, m, :], bank[:, m * S:(m + 1) * S], bqk[:, j, m:m + 1],
                                                      dst[HI][:, m, :], ALU.add, ALU.subtract)
            last.then_inc(made, 1)

        def add_self(i, now):
            dve.wait_ge(ctx_done[i], now)
            dve.wait_ge(diag_made[i], now)
            dve.wait_ge(proj_biased[i][SELF], now)
            nc.vector.scalar_tensor_tensor(ctx[i][:, :], proj[i][:, SELF, :], diag[i][:, :], b_ctx[:, 0:D],
                                           ALU.mult, ALU.add).then_inc(ctx_made[i], 1)

        def score_bias(r, now, before):
            dve.wait_ge(fills_made, 3)
            dve.wait_ge(s_done[r], now)
            dve.wait_ge(p_made[r], before)
            for k in range(KT):
                last = nc.vector.tensor_tensor_reduce(out=scores[:, r, k, :], in0=b_score[r][:, k * S:(k + 1) * S],
                                                      in1=adj_bias[:, :], scale=1.0, scalar=-3.0e38,
                                                      op0=ALU.add, op1=ALU.max, accum_out=s_max[:, r, k:k + 1])
            last.then_inc(s_made[r], 1)

        def score_nbias(r, now):
            dve.wait_ge(s_made[r], now)
            nc.vector.tensor_scalar(s_nbias[:, r, :], s_max[:, r, :], -A_SCALE, None,
                                    ALU.mult).then_inc(s_nbias_made[r], 1)

        def scale_ctx(i, now):
            dve.wait_ge(moments_made[i], now)
            nc.vector.scalar_tensor_tensor(scaled[i][:, :], ctx[i][:, :], mean_var[i][:, 0:1], gain[:, i, :],
                                           ALU.subtract, ALU.mult).then_inc(scaled_made[i], 1)

        def step(t, c, on):
            d = dma_counts(dve, t)
            if on[0]:
                dve.wait_ge(x_loaded[0], d[0])
                dve.wait_ge(h_made[0], c[1])
                moments(2, x_in[0], c[0])
            if on[1]:
                dve.wait_ge(proj_done[1][SELF], c[2])
                low_part(1, c[1])
            if on[0]:
                dve.wait_ge(rstd_made[2], c[0])
                dve.wait_ge(tr_done[0], c[1])
                nc.vector.tensor_scalar(h_rows[0][:, :], x_in[0][:, :], mean_var[2][:, 0:1], rstd[2][:, :],
                                        ALU.subtract, ALU.mult).then_inc(h_made[0], 1)
            if on[2]:
                dve.wait_ge(fills_made, 3)
                dve.wait_ge(adj_bias_made, c[2])
                score_bias(0, c[2], c[3])
            if on[1]:
                dve.wait_ge(e_made[1], c[2])
                max_u(1, c[1])
            if on[2]:
                score_nbias(0, c[2])
                score_bias(1, c[2], c[3])
            if on[1]:
                mask_delta(1, c[1], c[2], d[1])
            if on[2]:
                score_nbias(1, c[2])
                score_bias(2, c[2], c[3])
            if on[1]:
                take_diag(1, c[1])
            if on[2]:
                score_nbias(2, c[2])
                score_bias(3, c[2], c[3])
                score_nbias(3, c[2])
            if on[1]:
                mask_deltaT(1, c[1], c[2])
                bias_proj(1, RIGHT, c[1], ctx_done, c[2])
                bias_proj(1, SELF, c[1], ctx_made, c[2])
            if on[0]:
                dve.wait_ge(proj_done[0][SELF], c[1])
                low_part(0, c[0])
            if on[1]:
                dve.wait_ge(scaled_made[1], c[2])
                add_self(1, c[1])
            if on[1]:
                dve.wait_ge(ctx_made[1], c[1])
                moments(1, ctx[1], c[1])
            if on[0]:
                dve.wait_ge(e_made[0], c[1])
                max_u(0, c[0])
            if on[1]:
                scale_ctx(1, c[1])
            if on[0]:
                mask_delta(0, c[0], c[1], d[0])
            if on[1]:
                dve.wait_ge(scaled_made[1], c[1])
                dve.wait_ge(rstd_made[1], c[1])
                nc.vector.scalar_tensor_tensor(y_rows[:, :], scaled[1][:, :], rstd[1][:, :], shift[:, 1, :],
                                               ALU.mult, ALU.add).then_inc(y_made, 1)
            if on[1]:
                dve.wait_ge(y_made, c[1])
                dve.wait_ge(x_loaded[1], d[1])
                dve.wait_ge(x_bv_made, c[2])
                nc.vector.scalar_tensor_tensor(x_mid[:, :], y_rows[:, :], 0.0, x_in[1][:, :],
                                               ALU.max, ALU.add).then_inc(x_mid_made, 1)
                dve.wait_ge(x_mid_made, c[1])
                moments(3, x_mid, c[1])
            if on[0]:
                bias_proj(0, RIGHT, c[0], ctx_done, c[1])
            if on[1]:
                dve.wait_ge(rstd_made[3], c[1])
                dve.wait_ge(tr_done[2], c[2])
                nc.vector.tensor_scalar(h_rows[2][:, :], x_mid[:, :], mean_var[3][:, 0:1], rstd[3][:, :],
                                        ALU.subtract, ALU.mult).then_inc(h_made[2], 1)
            if on[0]:
                take_diag(0, c[0])
                mask_deltaT(0, c[0], c[1])
            if on[2]:
                dve.wait_ge(p_made[3], c[2])
                dve.wait_ge(att_made, c[3])
                nc.vector.reciprocal(p_recip[:, :, :], p_sum[:, :, :]).then_inc(recip_made, 1)
            if on[1]:
                dve.wait_ge(v_done, c[2])
                low_part(2, c[1])
            if on[2]:
                dve.wait_ge(recip_made, c[2])
                dve.wait_ge(o_done, c[2])
                dve.wait_ge(y_out_made, c[3])
                nc.vector.tensor_tensor(
                    att[:, :].rearrange("p (h d) -> p h d", d=HD), b_h[:, 0:D].rearrange("p (h d) -> p h d", d=HD),
                    p_recip[:, :, :].rearrange("p k (r o) -> p (k r) o", o=1).broadcast_to([128, HEADS, HD]),
                    ALU.mult).then_inc(att_made, 1)
            if on[0]:
                dve.wait_ge(scaled_made[0], c[1])
                add_self(0, c[0])
                dve.wait_ge(ctx_made[0], c[0])
                moments(0, ctx[0], c[0])
                scale_ctx(0, c[0])
            if on[1]:
                dve.wait_ge(s_done[1], c[2])
                low_columns(qT, b_c, 0, q_hi_made, q_made, c[1])
            if on[0]:
                dve.wait_ge(scaled_made[0], c[0])
                dve.wait_ge(rstd_made[0], c[0])
                dve.wait_ge(tr_done[1], c[1])
                nc.vector.scalar_tensor_tensor(o_rows[:, :], scaled[0][:, :], rstd[0][:, :], shift[:, 0, :],
                                               ALU.mult, ALU.add).then_inc(o_made, 1)
            if on[1]:
                low_columns(kT, b_d, 1, k_hi_made, k_made, c[1])

        dve.wait_ge(fills_made, 3)
        split_weights((LEFT, RIGHT, SELF))
        dve.wait_ge(consts_loaded, 16 * N_CONSTS)
        dve.wait_ge(scaled_consts_made, 3)
        run_steps(dve, step, between=lambda: split_weights(range(3, 9)))

    @block.gpsimd
    def _(pool):
        def bias_proj(i, m, now):
            pool.wait_ge(proj_copied[i][m], now)
            nc.gpsimd.tensor_tensor(proj[i][:, m, :], proj[i][:, m, :], bias3[:, i, m, :],
                                    ALU.add).then_inc(proj_biased[i][m], 1)

        def inverse_root(j, now):
            pool.wait_ge(veps_made[j], now)
            nc.gpsimd.tensor_tensor(rstd[j][:, :], var_eps[j][:, :], neg_half[:, :], ALU.pow).then_inc(rstd_made[j], 1)

        def norm_of(j, now):
            pool.wait_ge(fills_made, 3)
            pool.wait_ge(moments_made[j], now)
            nc.gpsimd.tensor_scalar(var_eps[j][:, :], mean_var[j][:, 1:2], LN_EPS, None, ALU.add).then_inc(veps_made[j], 1)
            inverse_root(j, now)

        def denominator(i, now):
            pool.wait_ge(fills_made, 3)
            pool.wait_ge(delta_made[i], now)
            nc.gpsimd.tensor_scalar(den[i][:, 0:1], e_sum[i][:, :], SUM_EPS, delta_sum[i][:, :],
                                    ALU.mult, ALU.add).then_inc(den_made[i], 1)
            pool.wait_ge(den_made[i], now)
            nc.gpsimd.tensor_tensor(den[i][:, 1:2], den[i][:, 0:1], den[i][:, 0:1], ALU.mult).then_inc(den_sq_made[i], 1)

        def norm_of_context(i, now):
            pool.wait_ge(fills_made, 3)
            pool.wait_ge(den_sq_made[i], now)
            pool.wait_ge(moments_made[i], now)
            nc.gpsimd.tensor_scalar(var_eps[i][:, :], den[i][:, 1:2], CTX_EPS * W_SCALE ** 2, mean_var[i][:, 1:2],
                                    ALU.mult, ALU.add).then_inc(veps_made[i], 1)
            inverse_root(i, now)

        def step(t, c, on):
            d = dma_counts(pool, t)
            if on[0]:
                norm_of(2, c[0])
            if on[1]:
                denominator(1, c[1])
                bias_proj(1, LEFT, c[1])
                norm_of_context(1, c[1])
            if on[0]:
                bias_proj(0, LEFT, c[0])
            if on[1]:
                norm_of(3, c[1])
            if on[0]:
                denominator(0, c[0])
                bias_proj(0, SELF, c[0])
            if on[2]:
                pool.wait_ge(att_made, c[2])
                pool.wait_ge(x_bv_made, c[2])
                pool.wait_ge(out_stored, d[3])
                nc.gpsimd.tensor_tensor(y_out[:, :], att[:, :], x_bv[:, :], ALU.add).then_inc(y_out_made, 1)
            if on[0]:
                norm_of_context(0, c[0])
            if on[1]:
                pool.wait_ge(y_out_made, c[2])
                nc.gpsimd.tensor_tensor(x_bv[:, :], x_mid[:, :], bv_rows[:, :], ALU.add).then_inc(x_bv_made, 1)
                pool.wait_ge(fills_made, 3)
                pool.wait_ge(adj_loaded[2], d[1])
                pool.wait_ge(s_made[3], c[2])
                nc.gpsimd.tensor_scalar(adj_cut[:, :], adj_in[2][:, :], 0.0, MASKED,
                                        ALU.is_le, ALU.mult).then_inc(cut_made, 1)
                nc.gpsimd.tensor_scalar(adj_beta[:, :], adj_in[2][:, :], beta_scaled[:, :], None,
                                        ALU.mult).then_inc(adj_beta_made, 1)
                pool.wait_ge(cut_made, c[1])
                pool.wait_ge(adj_beta_made, c[1])
                nc.gpsimd.tensor_tensor(adj_bias[:, :], adj_cut[:, :], adj_beta[:, :], ALU.add).then_inc(adj_bias_made, 1)

        nc.gpsimd.memset(ident[:, :], 0.0).then_inc(consts_made, 1)
        nc.gpsimd.memset(tri[:, :, :], 1.0).then_inc(consts_made, 1)
        nc.gpsimd.memset(neg_half[:, :], -0.5).then_inc(consts_made, 1)
        pool.wait_ge(consts_made, 3)
        nc.gpsimd.affine_select(out=ident[:, :], in_=ident[:, :], compare_op=ALU.not_equal, fill=1.0, base=0,
                                pattern=[[-1, 128]], channel_multiplier=1).then_inc(fills_made, 1)
        nc.gpsimd.affine_select(out=tri[:, 0, :], in_=tri[:, 0, :], compare_op=ALU.is_gt, fill=0.0, base=0,
                                pattern=[[-1, 128]], channel_multiplier=1).then_inc(fills_made, 1)
        nc.gpsimd.affine_select(out=tri[:, 1, :], in_=tri[:, 1, :], compare_op=ALU.is_gt, fill=0.0, base=0,
                                pattern=[[1, 128]], channel_multiplier=-1).then_inc(fills_made, 1)
        pool.wait_ge(consts_loaded, 16 * N_CONSTS)
        nc.gpsimd.tensor_scalar(beta_scaled[:, :], beta_col[:, :], 1.0 / A_SCALE, None, ALU.mult).then_inc(scaled_consts_made, 1)
        nc.gpsimd.tensor_scalar(bias3[:, :, :, :].rearrange("p l m n -> p (l m n)"),
                                bias3[:, :, :, :].rearrange("p l m n -> p (l m n)"), W_SCALE, None,
                                ALU.mult).then_inc(scaled_consts_made, 1)
        nc.gpsimd.tensor_scalar(bqk[:, :, :].rearrange("p j m -> p (j m)"), bqk[:, :, :].rearrange("p j m -> p (j m)"),
                                W_SCALE, None, ALU.mult).then_inc(scaled_consts_made, 1)
        pool.wait_ge(scaled_consts_made, 3)
        run_steps(pool, step)

    block.__exit__(None, None, None)


_INS = ["x", "adj", "L0_gnn_Wl", "L0_gnn_bl", "L0_gnn_Ws", "L0_gnn_bs", "L0_gnn_Wr", "L0_gnn_br",
        "L0_gnn_ln_w", "L0_gnn_ln_b", "L1_gnn_Wq", "L1_gnn_bq", "L1_gnn_Wk", "L1_gnn_bk",
        "L1_gnn_Wv", "L1_gnn_bv", "L1_gnn_beta"]
_TRANSPOSED = ("L0_gnn_Wl", "L0_gnn_Ws", "L0_gnn_Wr")


def kernel(**inputs):
    import concourse.bacc as bacc
    from concourse.bass_utils import run_bass_kernel_spmd

    nc = bacc.Bacc("TRN2", target_bir_lowering=False, num_devices=1)
    arrays, args = {}, []
    for name in _INS:
        a = np.asarray(inputs[name])
        if name in _TRANSPOSED:
            a = a.transpose(0, 2, 1)
        if a.ndim == 0:
            a = a.reshape(1, 1)
        a = np.ascontiguousarray(a)
        arrays[f"in_{name}"] = a
        args.append(nc.dram_tensor(f"in_{name}", a.shape, mybir.dt.from_np(a.dtype), kind="ExternalInput").ap())
    args.append(nc.dram_tensor("out_0", (ITEMS, S, D), F32, kind="ExternalOutput").ap())
    graph_block_program(nc, *args)
    r = run_bass_kernel_spmd(nc, [arrays], core_ids=[0])
    return r.results[0]["out_0"]
```

```python
import numpy as np

import concourse.bass as bass
from concourse import mybir
from concourse.alu_op_type import AluOpType as ALU

F32 = mybir.dt.float32
F16 = mybir.dt.float16
ACT = mybir.ActivationFunctionType
X_AXIS = mybir.AxisListType.X

ITEMS, S, D = 64, 128, 384
KT = D // 128
HEADS, HD = 12, 32
ROWS = 128 // HD
LN_EPS = 1e-5
CTX_EPS, SUM_EPS = 1e-12, 1e-10
U_SCALE = float(np.float32(1.0) / np.sqrt(np.float32(D)))
W_SCALE = 64.0
A_SCALE = float(np.float32(1.0) / np.sqrt(np.float32(HD)) / np.float32(W_SCALE ** 2))
MASKED = -(2.0 ** 80)
LEFT, SELF, RIGHT = range(3)
QW, KW, VW = 6, 7, 8
SPLIT_ORDER = (LEFT, RIGHT, SELF, 3 + LEFT, 3 + RIGHT, 3 + SELF, QW, KW, VW)
HI, LO = 0, 1


def graph_block_program(nc: bass.Bass, x, adj, wl, bl, ws, bs, wr, br, ln_w, ln_b,
                        wq, bq, wk, bk, wv, bv, beta, out):

    def sb(name, shape, dt=F32):
        return nc.alloc_sbuf_tensor(name, shape, dt)

    def sem(name, n=None):
        return nc.alloc_semaphore(name) if n is None else [nc.alloc_semaphore(f"{name}{i}") for i in range(n)]

    w_raw = sb("w_raw", [128, 9, KT, D])
    w_part = [sb("w_hi", [128, 9, KT, D], F16), sb("w_lo", [128, 9, KT, D], F16)]
    bias3 = sb("bias3", [128, 2, 3, D])
    gain, shift = sb("gain", [128, 2, D]), sb("shift", [128, 2, D])
    bv_rows = sb("bv_rows", [128, D])
    bqk = sb("bqk", [128, 2, KT])
    beta_col = sb("beta_col", [128, 1])
    beta_scaled = sb("beta_scaled", [128, 1])
    ident = sb("ident", [128, 128])
    tri = sb("tri", [128, 2, 128])
    neg_half = sb("neg_half", [128, 1])

    x_in = [sb("x_in0", [128, D]), sb("x_in1", [128, D])]
    adj_in = [sb(f"adj_in{i}", [128, S]) for i in range(3)]
    h_rows = [sb("h_rows0", [128, D]), None, sb("h_rows2", [128, D])]
    hT = [[sb(f"hT{i}_hi", [128, KT, S], F16), sb(f"hT{i}_lo", [128, KT, S], F16)] for i in range(3)]
    u_max, u_nbias = [sb(f"u_max{i}", [128, 1]) for i in range(2)], [sb(f"u_nbias{i}", [128, 1]) for i in range(2)]
    e_rows = [sb(f"e_rows{i}", [128, S]) for i in range(2)]
    e_sum = [sb(f"e_sum{i}", [128, 1]) for i in range(2)]
    delta = [sb(f"delta{i}", [128, S]) for i in range(2)]
    delta_sum = [sb(f"delta_sum{i}", [128, 1]) for i in range(2)]
    diag = [sb(f"diag{i}", [128, 1]) for i in range(2)]
    diag_junk = [sb(f"diag_junk{i}", [128, S]) for i in range(2)]
    deltaT = [sb(f"deltaT{i}", [128, 2, S]) for i in range(2)]
    proj = [sb(f"proj{i}", [128, 3, D]) for i in range(2)]
    ctx = [sb(f"ctx{i}", [128, D]) for i in range(2)]
    den = [sb(f"den{i}", [128, 2]) for i in range(2)]
    o_rows = sb("o_rows", [128, D])
    scaled = [sb("scaled0", [128, D]), sb("scaled1", [128, D])]
    y_rows = sb("y_rows", [128, D])
    x_mid = sb("x_mid", [128, D])
    stats = [sb(f"stats{i}", [128, 6]) for i in range(4)]
    mean_var = [sb(f"mean_var{i}", [128, 2]) for i in range(4)]
    var_eps = [sb(f"var_eps{i}", [128, 1]) for i in range(4)]
    rstd = [sb(f"rstd{i}", [128, 1]) for i in range(4)]

    qT = [sb("qT_hi", [128, KT, S], F16), sb("qT_lo", [128, KT, S], F16)]
    kT = [sb("kT_hi", [128, KT, S], F16), sb("kT_lo", [128, KT, S], F16)]
    v_rows = sb("v_rows", [128, D])
    adj_cut, adj_beta, adj_bias = sb("adj_cut", [128, S]), sb("adj_beta", [128, S]), sb("adj_bias", [128, S])
    scores = sb("scores", [128, ROWS, KT, S])
    s_max, s_nbias = sb("s_max", [128, ROWS, KT]), sb("s_nbias", [128, ROWS, KT])
    probs = sb("probs", [128, ROWS, KT, S])
    p_sum, p_recip = sb("p_sum", [128, KT, ROWS]), sb("p_recip", [128, KT, ROWS])
    probsT = sb("probsT", [128, ROWS, KT, S])
    oT = sb("oT", [128, KT, S])
    x_bv = sb("x_bv", [128, D])
    att = sb("att", [128, D])
    y_out = sb("y_out", [128, D])

    b_tr, b_u, b_c, b_d, b_e, b_ctx, b_g, b_h = [
        nc.alloc_psum_tensor(f"bank_{n}", [128, 512], F32) for n in ("tr", "u", "c", "d", "e", "ctx", "g", "h")]
    b_proj = [b_c, b_e, b_d]
    b_score = [b_d, b_e, b_g, b_h]
    b_pT = [b_g, b_h, b_g, b_h]

    def tiles(bank):
        return bank[:, 0:D].rearrange("p (t n) -> p t n", t=KT)

    w_loaded, w_hi_made, w_lo_made = sem("w_loaded", 9), sem("w_hi_made"), sem("w_lo_made")
    graph_consts_loaded, att_consts_loaded = sem("graph_consts_loaded", 2), sem("att_consts_loaded")
    memsets_made, fills_made = sem("memsets_made"), sem("fills_made")
    bias3_scaled, bqk_scaled, beta_scaled_made = sem("bias3_scaled"), sem("bqk_scaled"), sem("beta_scaled_made")
    x_loaded, adj_loaded = sem("x_loaded", 2), sem("adj_loaded", 3)
    out_stored = sem("out_stored")
    stats_made, moments_made = sem("stats_made", 4), sem("moments_made", 4)
    veps_made, rstd_made = sem("veps_made", 4), sem("rstd_made", 4)
    h_made = {0: sem("h_made0"), 2: sem("h_made2")}
    tr_done = sem("tr_done", 3)
    hT_hi_made, hT_lo_made = sem("hT_hi_made", 3), sem("hT_lo_made", 3)
    u_done, u_max_made, u_nbias_made = sem("u_done", 2), sem("u_max_made", 2), sem("u_nbias_made", 2)
    e_made, delta_made, diag_made = sem("e_made", 2), sem("delta_made", 2), sem("diag_made", 2)
    dT_done, dT_made = sem("dT_done", 2), sem("dT_made", 2)
    proj_done = [sem(f"proj_done{i}_", 3) for i in range(2)]
    proj_copied = [sem(f"proj_copied{i}_", 3) for i in range(2)]
    proj_biased = [sem(f"proj_biased{i}_", 3) for i in range(2)]
    ctx_done, ctx_made = sem("ctx_done", 2), sem("ctx_made", 2)
    den_made, den_sq_made = sem("den_made", 2), sem("den_sq_made", 2)
    scaled_made, o_made, y_made = sem("scaled_made", 2), sem("o_made"), sem("y_made")
    x_mid_made, x_bv_made = sem("x_mid_made"), sem("x_bv_made")
    q_done, k_done, v_done = sem("q_done"), sem("k_done"), sem("v_done")
    q_hi_made, k_hi_made = sem("q_hi_made"), sem("k_hi_made")
    q_made, k_made, v_made = sem("q_made"), sem("k_made"), sem("v_made")
    cut_made, adj_beta_made, adj_bias_made = sem("cut_made"), sem("adj_beta_made"), sem("adj_bias_made")
    s_done, s_made, s_nbias_made = sem("s_done", ROWS), sem("s_made", ROWS), sem("s_nbias_made", ROWS)
    p_made, pT_done, pT_made = sem("p_made", ROWS), sem("pT_done", ROWS), sem("pT_made", ROWS)
    pv_done, oT_made, o_done = sem("pv_done"), sem("oT_made"), sem("o_done")
    recip_made, att_made, y_out_made = sem("recip_made"), sem("att_made"), sem("y_out_made")

    def counts(eng, t):
        if isinstance(t, int):
            return [min(max(t + 1 - k, 0), ITEMS) for k in range(4)]
        return [eng.to_reg(t + 1), t, eng.to_reg(t - 1), eng.to_reg(t - 2)]

    def dma_counts(eng, t):
        if isinstance(t, int):
            return [16 * n for n in counts(eng, t)]
        return [eng.to_reg((t + 1) * 16), eng.to_reg(t * 16), eng.to_reg((t - 1) * 16), eng.to_reg((t - 2) * 16)]

    def is_step(t, n):
        return isinstance(t, int) and t == n

    def run_steps(eng, step):
        for t in range(3):
            step(t, counts(eng, t), (True, t >= 1, t >= 2))
        with eng.Fori(3, ITEMS) as t:
            step(t, counts(eng, t), (True, True, True))
        for t in range(ITEMS, ITEMS + 2):
            step(t, counts(eng, t), (False, t == ITEMS, True))

    block = nc.Block()
    block.__enter__()

    @block.sync
    def _(sp):
        w_src = [wl[0], ws[0], wr[0], wl[1], ws[1], wr[1], wq, wk, wv]

        def load_weight(n):
            sp.dma_start(w_raw[:, n], w_src[n].rearrange("(k p) n -> p k n", p=128)).then_inc(w_loaded[n], 16)

        def step(t, c, on):
            if on[0]:
                sp.wait_ge(h_made[0], c[1])
                sp.dma_start(x_in[0][:, :], x[bass.ds(t, 1)].rearrange("o s d -> (o s) d")).then_inc(x_loaded[0], 16)
                sp.wait_ge(delta_made[0], c[1])
                sp.dma_start(adj_in[0][:, :], adj[bass.ds(t, 1)].rearrange("o s d -> (o s) d")).then_inc(adj_loaded[0], 16)
            if is_step(t, 0):
                for n in (LEFT, RIGHT, SELF):
                    load_weight(n)
                load_graph_constants(0)
                for n in (3 + LEFT, 3 + RIGHT, 3 + SELF):
                    load_weight(n)
                load_graph_constants(1)
                for n in (QW, KW, VW):
                    load_weight(n)
                load_attention_constants()
            if on[1]:
                sp.wait_ge(delta_made[1], c[2])
                sp.dma_start(adj_in[1][:, :], adj[bass.ds(t - 1, 1)].rearrange("o s d -> (o s) d")).then_inc(adj_loaded[1], 16)
                sp.wait_ge(x_mid_made, c[2])
                sp.dma_start(x_in[1][:, :], x[bass.ds(t - 1, 1)].rearrange("o s d -> (o s) d")).then_inc(x_loaded[1], 16)
                sp.wait_ge(cut_made, c[2])
                sp.wait_ge(adj_beta_made, c[2])
                sp.dma_start(adj_in[2][:, :], adj[bass.ds(t - 1, 1)].rearrange("o s d -> (o s) d")).then_inc(adj_loaded[2], 16)

        def load_graph_constants(l):
            for m, b in ((LEFT, bl), (RIGHT, br), (SELF, bs)):
                sp.dma_start(bias3[:, l, m, :], row(b, l)).then_inc(graph_consts_loaded[l], 16)
            for dst, src in ((gain, ln_w), (shift, ln_b)):
                sp.dma_start(dst[:, l, :], row(src, l)).then_inc(graph_consts_loaded[l], 16)

        def load_attention_constants():
            sp.dma_start(bv_rows[:, :], bv.rearrange("(o n) -> o n", o=1).broadcast_to([128, D])).then_inc(att_consts_loaded, 16)
            with nc.allow_non_contiguous_dma(reason="two small bias columns"):
                sp.dma_start(bqk[:, 0, :], bq.rearrange("(t p) -> p t", p=128)).then_inc(att_consts_loaded, 16)
                sp.dma_start(bqk[:, 1, :], bk.rearrange("(t p) -> p t", p=128)).then_inc(att_consts_loaded, 16)
            sp.dma_start(beta_col[:, :], beta.broadcast_to([128, 1])).then_inc(att_consts_loaded, 16)

        def row(a, l):
            return a[l:l + 1, :].broadcast_to([128, D])

        run_steps(sp, step)
        sp.wait_ge(out_stored, 16 * ITEMS)

    N_GRAPH_CONSTS, N_ATT_CONSTS = 5, 4

    @block.tensor
    def _(pe):
        def transpose_rows(src, last_sem):
            for k in range(KT):
                last = nc.tensor.transpose(b_tr[:, k * S:(k + 1) * S], src[:, k * 128:(k + 1) * 128], ident[:, :])
            last.then_inc(last_sem, 1)

        def project_rows(bank, i, n, done):
            pe.wait_ge(w_lo_made, SPLIT_ORDER.index(n) + 1)
            for k in range(KT):
                for a, b in ((HI, HI), (HI, LO), (LO, HI)):
                    last = nc.tensor.matmul(bank[:, 0:D], hT[i][a][:, k, :], w_part[b][:, n, k, :],
                                            start=(k == 0 and (a, b) == (HI, HI)),
                                            stop=(k == KT - 1 and (a, b) == (LO, HI)))
            last.then_inc(done, 1)

        def project_columns(bank, i, n, done):
            pe.wait_ge(w_lo_made, SPLIT_ORDER.index(n) + 1)
            for m in range(KT):
                for k in range(KT):
                    for a, b in ((HI, HI), (HI, LO), (LO, HI)):
                        last = nc.tensor.matmul(bank[:, m * S:(m + 1) * S],
                                                w_part[a][:, n, k, m * 128:(m + 1) * 128], hT[i][b][:, k, :],
                                                start=(k == 0 and (a, b) == (HI, HI)),
                                                stop=(k == KT - 1 and (a, b) == (LO, HI)))
            last.then_inc(done, 1)

        def similarity(i):
            for k in range(KT):
                for a, b in ((HI, HI), (HI, LO), (LO, HI)):
                    last = nc.tensor.matmul(b_u[:, 0:S], hT[i][a][:, k, :], hT[i][b][:, k, :],
                                            start=(k == 0 and (a, b) == (HI, HI)),
                                            stop=(k == KT - 1 and (a, b) == (LO, HI)))
            last.then_inc(u_done[i], 1)

        def transpose_delta(i):
            nc.tensor.transpose(b_u[:, S:2 * S], delta[i][:, :], ident[:, :]).then_inc(dT_done[i], 1)

        def context(i):
            nc.tensor.matmul(b_ctx[:, 0:D], deltaT[i][:, 0, :], proj[i][:, LEFT, :], start=True, stop=False)
            nc.tensor.matmul(b_ctx[:, 0:D], deltaT[i][:, 1, :], proj[i][:, RIGHT, :], start=False,
                             stop=True).then_inc(ctx_done[i], 1)

        def transpose_probs(r):
            for k in range(KT):
                last = nc.tensor.transpose(b_pT[r][:, k * S:(k + 1) * S], probs[:, r, k, :], ident[:, :])
            last.then_inc(pT_done[r], 1)

        def apply_probs(k):
            for r in range(ROWS):
                h = k * ROWS + r
                last = nc.tensor.matmul(b_g[r * HD:(r + 1) * HD, k * S:(k + 1) * S], v_rows[:, h * HD:(h + 1) * HD],
                                        probsT[:, r, k, :], start=True, stop=True)
            return last

        def scores_of(k, quads):
            for a, b in ((HI, HI), (HI, LO), (LO, HI)):
                for r in quads:
                    quad = slice(r * HD, (r + 1) * HD)
                    last = nc.tensor.matmul(b_score[r][:, k * S:(k + 1) * S], qT[a][quad, k, :], kT[b][quad, k, :],
                                            start=((a, b) == (HI, HI)), stop=((a, b) == (LO, HI)))
                    if k == KT - 1 and (a, b) == (LO, HI):
                        last.then_inc(s_done[r], 1)

        def step(t, c, on):
            if on[2]:
                pe.wait_ge(q_made, c[2])
                pe.wait_ge(k_made, c[2])
                pe.wait_ge(oT_made, c[3])
                scores_of(0, (0, 2, 3))
                pe.wait_ge(v_made, c[2])
                scores_of(0, (1,))
                scores_of(1, (0, 2, 3, 1))
                scores_of(2, (0, 2, 3, 1))
            if on[1]:
                pe.wait_ge(hT_lo_made[1], c[1])
                pe.wait_ge(dT_made[0], c[1])
                similarity(1)
                pe.wait_ge(q_made, c[2])
                project_rows(b_c, 1, 3 + LEFT, proj_done[1][LEFT])
                pe.wait_ge(k_made, c[2])
                pe.wait_ge(s_made[0], c[2])
                project_rows(b_d, 1, 3 + RIGHT, proj_done[1][RIGHT])
                pe.wait_ge(delta_made[1], c[1])
                transpose_delta(1)
                pe.wait_ge(s_made[1], c[2])
                pe.wait_ge(proj_copied[0][SELF], c[1])
                project_rows(b_e, 1, 3 + SELF, proj_done[1][SELF])
            if on[0]:
                pe.wait_ge(h_made[0], c[0])
                pe.wait_ge(hT_lo_made[1], c[1])
                transpose_rows(h_rows[0], tr_done[0])
            if on[1]:
                pe.wait_ge(dT_made[1], c[1])
                pe.wait_ge(proj_biased[1][LEFT], c[1])
                pe.wait_ge(proj_biased[1][RIGHT], c[1])
                pe.wait_ge(ctx_made[0], c[1])
                pe.wait_ge(att_made, c[3])
                context(1)
            if on[2]:
                pe.wait_ge(p_made[0], c[2])
                pe.wait_ge(s_made[2], c[2])
                transpose_probs(0)
                pe.wait_ge(p_made[1], c[2])
                pe.wait_ge(s_made[3], c[2])
                transpose_probs(1)
            if on[0]:
                pe.wait_ge(hT_lo_made[0], c[0])
                pe.wait_ge(dT_made[1], c[1])
                similarity(0)
                pe.wait_ge(proj_copied[1][LEFT], c[1])
                project_rows(b_c, 0, LEFT, proj_done[0][LEFT])
            if on[2]:
                pe.wait_ge(p_made[2], c[2])
                pe.wait_ge(pT_made[0], c[2])
                transpose_probs(2)
                pe.wait_ge(p_made[3], c[2])
                pe.wait_ge(pT_made[1], c[2])
                transpose_probs(3)
            if on[0]:
                pe.wait_ge(proj_biased[1][RIGHT], c[1])
                project_rows(b_d, 0, RIGHT, proj_done[0][RIGHT])
            if on[2]:
                pe.wait_ge(v_made, c[2])
                for r in range(ROWS):
                    pe.wait_ge(pT_made[r], c[2])
                apply_probs(0)
                apply_probs(1)
            if on[0]:
                pe.wait_ge(delta_made[0], c[0])
                transpose_delta(0)
                pe.wait_ge(proj_biased[1][SELF], c[1])
                project_rows(b_e, 0, SELF, proj_done[0][SELF])
            if on[1]:
                pe.wait_ge(h_made[2], c[1])
                pe.wait_ge(hT_lo_made[0], c[0])
                transpose_rows(h_rows[2], tr_done[2])
            if on[2]:
                apply_probs(2).then_inc(pv_done, 1)
            if on[0]:
                pe.wait_ge(dT_made[0], c[0])
                pe.wait_ge(proj_biased[0][LEFT], c[0])
                pe.wait_ge(proj_biased[0][RIGHT], c[0])
                pe.wait_ge(ctx_made[1], c[1])
                context(0)
            if on[1]:
                pe.wait_ge(hT_lo_made[2], c[1])
                pe.wait_ge(proj_copied[0][LEFT], c[0])
                project_columns(b_c, 2, QW, q_done)
                pe.wait_ge(proj_biased[0][RIGHT], c[0])
                project_columns(b_d, 2, KW, k_done)
                pe.wait_ge(proj_copied[0][SELF], c[0])
                project_rows(b_e, 2, VW, v_done)
            if on[0]:
                pe.wait_ge(o_made, c[0])
                pe.wait_ge(hT_lo_made[2], c[1])
                transpose_rows(o_rows, tr_done[1])
            if on[2]:
                pe.wait_ge(oT_made, c[2])
                pe.wait_ge(ctx_made[0], c[0])
                for k in range(KT):
                    last = nc.tensor.transpose(b_ctx[:, k * 128:(k + 1) * 128], oT[:, k, :], ident[:, :])
                last.then_inc(o_done, 1)

        pe.wait_ge(fills_made, 3)
        run_steps(pe, step)

    @block.scalar
    def _(act):
        def split_weights(names):
            for n in names:
                act.wait_ge(w_loaded[n], 16)
                nc.scalar.activation(w_part[HI][:, n], w_raw[:, n], ACT.Copy, scale=W_SCALE).then_inc(w_hi_made, 1)

        def high_part(i, now):
            act.wait_ge(tr_done[i], now)
            nc.scalar.activation(hT[i][HI][:, :, :], tiles(b_tr), ACT.Relu).then_inc(hT_hi_made[i], 1)

        def exp_u(i, now):
            act.wait_ge(u_nbias_made[i], now)
            nc.scalar.activation(e_rows[i][:, :], b_u[:, 0:S], ACT.Exp, bias=u_nbias[i][:, :], scale=U_SCALE,
                                 accum_out=e_sum[i][:, :]).then_inc(e_made[i], 1)

        def copy_proj(i, m, now):
            act.wait_ge(proj_done[i][m], now)
            nc.scalar.activation(proj[i][:, m, :], b_proj[m][:, 0:D], ACT.Copy).then_inc(proj_copied[i][m], 1)

        def exp_scores(r, now, before):
            act.wait_ge(s_nbias_made[r], now)
            act.wait_ge(pT_done[r], before)
            for k in range(KT):
                last = nc.scalar.activation(probs[:, r, k, :], scores[:, r, k, :], ACT.Exp,
                                            bias=s_nbias[:, r, k:k + 1], scale=A_SCALE,
                                            accum_out=p_sum[:, k, r:r + 1])
            last.then_inc(p_made[r], 1)

        def copy_pT(r, now, before):
            act.wait_ge(pT_done[r], now)
            act.wait_ge(pv_done, before)
            nc.scalar.activation(probsT[:, r, :, :], tiles(b_pT[r]), ACT.Copy).then_inc(pT_made[r], 1)

        def step(t, c, on):
            if on[1]:
                act.wait_ge(delta_made[1], c[2])
                act.wait_ge(den_made[1], c[2])
                exp_u(1, c[1])
            if on[2]:
                act.wait_ge(recip_made, c[3])
                exp_scores(0, c[2], c[3])
            if on[1]:
                act.wait_ge(ctx_done[1], c[2])
                copy_proj(1, LEFT, c[1])
            if is_step(t, 1):
                split_weights((KW, VW))
                act.wait_ge(att_consts_loaded, 16 * N_ATT_CONSTS)
                nc.scalar.activation(bqk[:, :, :], bqk[:, :, :], ACT.Copy, scale=W_SCALE).then_inc(bqk_scaled, 1)
                act.wait_ge(bqk_scaled, 1)
            if on[2]:
                exp_scores(1, c[2], c[3])
                exp_scores(2, c[2], c[3])
            if on[0]:
                act.wait_ge(proj_done[0][SELF], c[1])
                high_part(0, c[0])
            if is_step(t, 0):
                split_weights((RIGHT, SELF))
            if on[2]:
                exp_scores(3, c[2], c[3])
                copy_pT(0, c[2], c[3])
                copy_pT(1, c[2], c[3])
            if on[0]:
                act.wait_ge(delta_made[0], c[1])
                act.wait_ge(den_made[0], c[1])
                exp_u(0, c[0])
            if is_step(t, 0):
                scale_bias3(0)
            if on[0]:
                act.wait_ge(ctx_done[0], c[1])
                copy_proj(0, LEFT, c[0])
            if is_step(t, 0):
                split_weights((3 + LEFT, 3 + RIGHT))
            if on[2]:
                copy_pT(2, c[2], c[3])
                copy_pT(3, c[2], c[3])
            if on[0]:
                act.wait_ge(ctx_made[0], c[1])
                copy_proj(0, SELF, c[0])
            if is_step(t, 0):
                split_weights((3 + SELF,))
                scale_bias3(1)
            if on[1]:
                act.wait_ge(v_done, c[2])
                high_part(2, c[1])
            if on[2]:
                act.wait_ge(pv_done, c[2])
                act.wait_ge(o_done, c[3])
                nc.scalar.activation(oT[:, :, :], tiles(b_g), ACT.Copy).then_inc(oT_made, 1)
            if on[1]:
                for dst, bank, j, done, made in ((qT, b_c, 0, q_done, q_hi_made), (kT, b_d, 1, k_done, k_hi_made)):
                    act.wait_ge(done, c[1])
                    act.wait_ge(s_done[1], c[2])
                    for m in range(KT):
                        last = nc.scalar.activation(dst[HI][:, m, :], bank[:, m * S:(m + 1) * S], ACT.Identity,
                                                    bias=bqk[:, j, m:m + 1])
                    last.then_inc(made, 1)
                act.wait_ge(v_done, c[1])
                act.wait_ge(pv_done, c[2])
                nc.scalar.activation(v_rows[:, :], b_e[:, 0:D], ACT.Copy, scale=1.0 / W_SCALE).then_inc(v_made, 1)
            if on[0]:
                act.wait_ge(proj_done[1][SELF], c[1])
                high_part(1, c[0])
            if is_step(t, 0):
                split_weights((QW,))
            if on[2]:
                act.wait_ge(y_out_made, c[2])
                act.dma_start(out[bass.ds(t - 2, 1)].rearrange("o s d -> (o s) d"), y_out[:, :]).then_inc(out_stored, 16)

        def scale_bias3(l):
            act.wait_ge(graph_consts_loaded[l], 16 * N_GRAPH_CONSTS)
            nc.scalar.activation(bias3[:, l, :, :], bias3[:, l, :, :], ACT.Copy, scale=W_SCALE).then_inc(bias3_scaled, 1)

        split_weights((LEFT,))
        run_steps(act, step)

    @block.vector
    def _(dve):
        def split_weights(names):
            for n in names:
                dve.wait_ge(w_hi_made, SPLIT_ORDER.index(n) + 1)
                nc.vector.scalar_tensor_tensor(w_part[LO][:, n], w_raw[:, n], W_SCALE, w_part[HI][:, n],
                                               ALU.mult, ALU.subtract).then_inc(w_lo_made, 1)

        def moments(j, src, now):
            nc.vector.bn_stats(stats[j][:, :], src[:, :]).then_inc(stats_made[j], 1)
            dve.wait_ge(fills_made, 3)
            dve.wait_ge(stats_made[j], now)
            nc.vector.bn_aggr(mean_var[j][:, :], stats[j][:, :]).then_inc(moments_made[j], 1)

        def low_part(i, now):
            dve.wait_ge(hT_hi_made[i], now)
            nc.vector.scalar_tensor_tensor(hT[i][LO][:, :, :], tiles(b_tr), 0.0, hT[i][HI][:, :, :],
                                           ALU.max, ALU.subtract).then_inc(hT_lo_made[i], 1)

        def max_u(i, now):
            dve.wait_ge(u_done[i], now)
            nc.vector.reduce_max(u_max[i][:, :], b_u[:, 0:S], X_AXIS).then_inc(u_max_made[i], 1)
            dve.wait_ge(u_max_made[i], now)
            nc.vector.tensor_scalar(u_nbias[i][:, :], u_max[i][:, :], -U_SCALE, None,
                                    ALU.mult).then_inc(u_nbias_made[i], 1)

        def mask_delta(i, now, before, dma_now):
            dve.wait_ge(e_made[i], now)
            dve.wait_ge(adj_loaded[i], dma_now)
            dve.wait_ge(dT_done[i], before)
            dve.wait_ge(den_made[i], before)
            nc.vector.tensor_tensor_reduce(out=delta[i][:, :], in0=e_rows[i][:, :], in1=adj_in[i][:, :], scale=1.0,
                                           scalar=0.0, op0=ALU.mult, op1=ALU.add,
                                           accum_out=delta_sum[i][:, :]).then_inc(delta_made[i], 1)

        def take_diag(i, now):
            dve.wait_ge(delta_made[i], now)
            nc.vector.tensor_tensor_reduce(out=diag_junk[i][:, :], in0=delta[i][:, :], in1=ident[:, :], scale=1.0,
                                           scalar=0.0, op0=ALU.mult, op1=ALU.add,
                                           accum_out=diag[i][:, :]).then_inc(diag_made[i], 1)

        def mask_deltaT(i, now, before):
            dve.wait_ge(dT_done[i], now)
            dve.wait_ge(ctx_done[i], before)
            both = b_u[:, S:2 * S].rearrange("p (o n) -> p o n", o=1).broadcast_to([128, 2, S])
            nc.vector.tensor_tensor(deltaT[i][:, :, :], both, tri[:, :, :], ALU.mult).then_inc(dT_made[i], 1)

        def bias_proj(i, m, now, used, before):
            dve.wait_ge(proj_done[i][m], now)
            dve.wait_ge(used[i], before)
            nc.vector.tensor_tensor(proj[i][:, m, :], b_proj[m][:, 0:D], bias3[:, i, m, :],
                                    ALU.add).then_inc(proj_biased[i][m], 1)

        def low_columns(dst, bank, j, hi_made, made, now):
            dve.wait_ge(hi_made, now)
            for m in range(KT):
                last = nc.vector.scalar_tensor_tensor(dst[LO][:, m, :], bank[:, m * S:(m + 1) * S], bqk[:, j, m:m + 1],
                                                      dst[HI][:, m, :], ALU.add, ALU.subtract)
            last.then_inc(made, 1)

        def add_self(i, now):
            dve.wait_ge(ctx_done[i], now)
            dve.wait_ge(diag_made[i], now)
            dve.wait_ge(proj_biased[i][SELF], now)
            nc.vector.scalar_tensor_tensor(ctx[i][:, :], proj[i][:, SELF, :], diag[i][:, :], b_ctx[:, 0:D],
                                           ALU.mult, ALU.add).then_inc(ctx_made[i], 1)

        def score_bias(r, now, before):
            dve.wait_ge(fills_made, 3)
            dve.wait_ge(s_done[r], now)
            dve.wait_ge(p_made[r], before)
            for k in range(KT):
                last = nc.vector.tensor_tensor_reduce(out=scores[:, r, k, :], in0=b_score[r][:, k * S:(k + 1) * S],
                                                      in1=adj_bias[:, :], scale=1.0, scalar=-3.0e38,
                                                      op0=ALU.add, op1=ALU.max, accum_out=s_max[:, r, k:k + 1])
            last.then_inc(s_made[r], 1)

        def score_nbias(r, now):
            dve.wait_ge(s_made[r], now)
            nc.vector.tensor_scalar(s_nbias[:, r, :], s_max[:, r, :], -A_SCALE, None,
                                    ALU.mult).then_inc(s_nbias_made[r], 1)

        def scale_ctx(i, now):
            dve.wait_ge(moments_made[i], now)
            nc.vector.scalar_tensor_tensor(scaled[i][:, :], ctx[i][:, :], mean_var[i][:, 0:1], gain[:, i, :],
                                           ALU.subtract, ALU.mult).then_inc(scaled_made[i], 1)

        def step(t, c, on):
            d = dma_counts(dve, t)
            if on[1]:
                dve.wait_ge(proj_done[1][SELF], c[2])
                low_part(1, c[1])
            if is_step(t, 1):
                split_weights((3 + SELF,))
            if on[0]:
                dve.wait_ge(x_loaded[0], d[0])
                dve.wait_ge(h_made[0], c[1])
                moments(2, x_in[0], c[0])
            if on[2]:
                dve.wait_ge(fills_made, 3)
                dve.wait_ge(adj_bias_made, c[2])
                score_bias(0, c[2], c[3])
            if on[1]:
                dve.wait_ge(e_made[1], c[2])
                max_u(1, c[1])
            if on[2]:
                score_nbias(0, c[2])
                score_bias(1, c[2], c[3])
            if on[1]:
                mask_delta(1, c[1], c[2], d[1])
            if on[0]:
                dve.wait_ge(rstd_made[2], c[0])
                dve.wait_ge(tr_done[0], c[1])
                nc.vector.tensor_scalar(h_rows[0][:, :], x_in[0][:, :], mean_var[2][:, 0:1], rstd[2][:, :],
                                        ALU.subtract, ALU.mult).then_inc(h_made[0], 1)
            if on[2]:
                score_nbias(1, c[2])
                score_bias(2, c[2], c[3])
            if is_step(t, 1):
                dve.wait_ge(bias3_scaled, 2)
                split_weights((QW, KW, VW))
            if on[1]:
                take_diag(1, c[1])
            if on[2]:
                score_nbias(2, c[2])
            if on[1]:
                mask_deltaT(1, c[1], c[2])
                bias_proj(1, RIGHT, c[1], ctx_done, c[2])
            if on[2]:
                score_bias(3, c[2], c[3])
                score_nbias(3, c[2])
            if on[1]:
                bias_proj(1, SELF, c[1], ctx_made, c[2])
            if is_step(t, 0):
                split_weights((LEFT,))
            if on[0]:
                dve.wait_ge(proj_done[0][SELF], c[1])
                low_part(0, c[0])
            if is_step(t, 0):
                split_weights((RIGHT, SELF))
            if on[1]:
                dve.wait_ge(scaled_made[1], c[2])
                add_self(1, c[1])
                dve.wait_ge(ctx_made[1], c[1])
                moments(1, ctx[1], c[1])
            if on[0]:
                dve.wait_ge(e_made[0], c[1])
                max_u(0, c[0])
            if on[1]:
                scale_ctx(1, c[1])
            if on[0]:
                mask_delta(0, c[0], c[1], d[0])
            if on[1]:
                dve.wait_ge(scaled_made[1], c[1])
                dve.wait_ge(rstd_made[1], c[1])
                nc.vector.scalar_tensor_tensor(y_rows[:, :], scaled[1][:, :], rstd[1][:, :], shift[:, 1, :],
                                               ALU.mult, ALU.add).then_inc(y_made, 1)
                dve.wait_ge(y_made, c[1])
                dve.wait_ge(x_loaded[1], d[1])
                dve.wait_ge(x_bv_made, c[2])
                nc.vector.scalar_tensor_tensor(x_mid[:, :], y_rows[:, :], 0.0, x_in[1][:, :],
                                               ALU.max, ALU.add).then_inc(x_mid_made, 1)
                dve.wait_ge(x_mid_made, c[1])
                moments(3, x_mid, c[1])
            if on[0]:
                if is_step(t, 0):
                    dve.wait_ge(bias3_scaled, 1)
                bias_proj(0, RIGHT, c[0], ctx_done, c[1])
            if on[1]:
                dve.wait_ge(rstd_made[3], c[1])
                dve.wait_ge(tr_done[2], c[2])
                nc.vector.tensor_scalar(h_rows[2][:, :], x_mid[:, :], mean_var[3][:, 0:1], rstd[3][:, :],
                                        ALU.subtract, ALU.mult).then_inc(h_made[2], 1)
            if on[0]:
                take_diag(0, c[0])
                mask_deltaT(0, c[0], c[1])
            if is_step(t, 0):
                split_weights((3 + LEFT,))
            if on[2]:
                dve.wait_ge(p_made[3], c[2])
                dve.wait_ge(att_made, c[3])
                nc.vector.reciprocal(p_recip[:, :, :], p_sum[:, :, :]).then_inc(recip_made, 1)
            if on[1]:
                dve.wait_ge(v_done, c[2])
                low_part(2, c[1])
            if on[0]:
                dve.wait_ge(scaled_made[0], c[1])
                add_self(0, c[0])
                dve.wait_ge(ctx_made[0], c[0])
                moments(0, ctx[0], c[0])
                scale_ctx(0, c[0])
            if on[1]:
                dve.wait_ge(s_done[1], c[2])
                if is_step(t, 1):
                    dve.wait_ge(bqk_scaled, 1)
                low_columns(qT, b_c, 0, q_hi_made, q_made, c[1])
            if on[0]:
                dve.wait_ge(scaled_made[0], c[0])
                dve.wait_ge(rstd_made[0], c[0])
                dve.wait_ge(tr_done[1], c[1])
                nc.vector.scalar_tensor_tensor(o_rows[:, :], scaled[0][:, :], rstd[0][:, :], shift[:, 0, :],
                                               ALU.mult, ALU.add).then_inc(o_made, 1)
            if is_step(t, 0):
                split_weights((3 + RIGHT,))
            if on[1]:
                low_columns(kT, b_d, 1, k_hi_made, k_made, c[1])
            if on[2]:
                dve.wait_ge(recip_made, c[2])
                dve.wait_ge(o_done, c[2])
                dve.wait_ge(y_out_made, c[3])
                nc.vector.tensor_tensor(
                    att[:, :].rearrange("p (h d) -> p h d", d=HD), b_ctx[:, 0:D].rearrange("p (h d) -> p h d", d=HD),
                    p_recip[:, :, :].rearrange("p k (r o) -> p (k r) o", o=1).broadcast_to([128, HEADS, HD]),
                    ALU.mult).then_inc(att_made, 1)

        dve.wait_ge(fills_made, 3)
        run_steps(dve, step)

    @block.gpsimd
    def _(pool):
        def bias_proj(i, m, now):
            pool.wait_ge(proj_copied[i][m], now)
            nc.gpsimd.tensor_tensor(proj[i][:, m, :], proj[i][:, m, :], bias3[:, i, m, :],
                                    ALU.add).then_inc(proj_biased[i][m], 1)

        def inverse_root(j, now):
            pool.wait_ge(veps_made[j], now)
            nc.gpsimd.tensor_tensor(rstd[j][:, :], var_eps[j][:, :], neg_half[:, :], ALU.pow).then_inc(rstd_made[j], 1)

        def norm_of(j, now):
            pool.wait_ge(fills_made, 3)
            pool.wait_ge(moments_made[j], now)
            nc.gpsimd.tensor_scalar(var_eps[j][:, :], mean_var[j][:, 1:2], LN_EPS, None, ALU.add).then_inc(veps_made[j], 1)
            inverse_root(j, now)

        def denominator(i, now):
            pool.wait_ge(fills_made, 3)
            pool.wait_ge(delta_made[i], now)
            nc.gpsimd.tensor_scalar(den[i][:, 0:1], e_sum[i][:, :], SUM_EPS, delta_sum[i][:, :],
                                    ALU.mult, ALU.add).then_inc(den_made[i], 1)
            pool.wait_ge(den_made[i], now)
            nc.gpsimd.tensor_tensor(den[i][:, 1:2], den[i][:, 0:1], den[i][:, 0:1], ALU.mult).then_inc(den_sq_made[i], 1)

        def norm_of_context(i, now):
            pool.wait_ge(fills_made, 3)
            pool.wait_ge(den_sq_made[i], now)
            pool.wait_ge(moments_made[i], now)
            nc.gpsimd.tensor_scalar(var_eps[i][:, :], den[i][:, 1:2], CTX_EPS * W_SCALE ** 2, mean_var[i][:, 1:2],
                                    ALU.mult, ALU.add).then_inc(veps_made[i], 1)
            inverse_root(i, now)

        def step(t, c, on):
            d = dma_counts(pool, t)
            if on[0]:
                norm_of(2, c[0])
            if on[2]:
                pool.wait_ge(y_out_made, c[3])
                pool.wait_ge(x_mid_made, c[2])
                nc.gpsimd.tensor_tensor(x_bv[:, :], x_mid[:, :], bv_rows[:, :], ALU.add).then_inc(x_bv_made, 1)
            if on[1]:
                denominator(1, c[1])
                if is_step(t, 1):
                    pool.wait_ge(bias3_scaled, 2)
                bias_proj(1, LEFT, c[1])
                norm_of_context(1, c[1])
            if is_step(t, 0):
                pool.wait_ge(bias3_scaled, 1)
            if on[0]:
                bias_proj(0, LEFT, c[0])
            if on[1]:
                norm_of(3, c[1])
            if on[0]:
                denominator(0, c[0])
                bias_proj(0, SELF, c[0])
                norm_of_context(0, c[0])
            if on[1]:
                if is_step(t, 1):
                    pool.wait_ge(att_consts_loaded, 16 * N_ATT_CONSTS)
                    nc.gpsimd.tensor_scalar(beta_scaled[:, :], beta_col[:, :], 1.0 / A_SCALE, None,
                                            ALU.mult).then_inc(beta_scaled_made, 1)
                    pool.wait_ge(beta_scaled_made, 1)
                pool.wait_ge(fills_made, 3)
                pool.wait_ge(adj_loaded[2], d[1])
                pool.wait_ge(s_made[3], c[2])
                nc.gpsimd.tensor_scalar(adj_cut[:, :], adj_in[2][:, :], 0.0, MASKED,
                                        ALU.is_le, ALU.mult).then_inc(cut_made, 1)
                nc.gpsimd.tensor_scalar(adj_beta[:, :], adj_in[2][:, :], beta_scaled[:, :], None,
                                        ALU.mult).then_inc(adj_beta_made, 1)
                pool.wait_ge(cut_made, c[1])
                pool.wait_ge(adj_beta_made, c[1])
                nc.gpsimd.tensor_tensor(adj_bias[:, :], adj_cut[:, :], adj_beta[:, :], ALU.add).then_inc(adj_bias_made, 1)
            if on[2]:
                pool.wait_ge(att_made, c[2])
                pool.wait_ge(x_bv_made, c[2])
                pool.wait_ge(out_stored, d[3])
                nc.gpsimd.tensor_tensor(y_out[:, :], att[:, :], x_bv[:, :], ALU.add).then_inc(y_out_made, 1)

        nc.gpsimd.memset(ident[:, :], 0.0).then_inc(memsets_made, 1)
        nc.gpsimd.memset(tri[:, :, :], 1.0).then_inc(memsets_made, 1)
        nc.gpsimd.memset(neg_half[:, :], -0.5).then_inc(memsets_made, 1)
        pool.wait_ge(memsets_made, 3)
        nc.gpsimd.affine_select(out=ident[:, :], in_=ident[:, :], compare_op=ALU.not_equal, fill=1.0, base=0,
                                pattern=[[-1, 128]], channel_multiplier=1).then_inc(fills_made, 1)
        nc.gpsimd.affine_select(out=tri[:, 0, :], in_=tri[:, 0, :], compare_op=ALU.is_gt, fill=0.0, base=0,
                                pattern=[[-1, 128]], channel_multiplier=1).then_inc(fills_made, 1)
        nc.gpsimd.affine_select(out=tri[:, 1, :], in_=tri[:, 1, :], compare_op=ALU.is_gt, fill=0.0, base=0,
                                pattern=[[1, 128]], channel_multiplier=-1).then_inc(fills_made, 1)
        run_steps(pool, step)

    block.__exit__(None, None, None)


_INS = ["x", "adj", "L0_gnn_Wl", "L0_gnn_bl", "L0_gnn_Ws", "L0_gnn_bs", "L0_gnn_Wr", "L0_gnn_br",
        "L0_gnn_ln_w", "L0_gnn_ln_b", "L1_gnn_Wq", "L1_gnn_bq", "L1_gnn_Wk", "L1_gnn_bk",
        "L1_gnn_Wv", "L1_gnn_bv", "L1_gnn_beta"]
_TRANSPOSED = ("L0_gnn_Wl", "L0_gnn_Ws", "L0_gnn_Wr")


def kernel(**inputs):
    import concourse.bacc as bacc
    from concourse.bass_utils import run_bass_kernel_spmd

    nc = bacc.Bacc("TRN2", target_bir_lowering=False, num_devices=1)
    arrays, args = {}, []
    for name in _INS:
        a = np.asarray(inputs[name])
        if name in _TRANSPOSED:
            a = a.transpose(0, 2, 1)
        if a.ndim == 0:
            a = a.reshape(1, 1)
        a = np.ascontiguousarray(a)
        arrays[f"in_{name}"] = a
        args.append(nc.dram_tensor(f"in_{name}", a.shape, mybir.dt.from_np(a.dtype), kind="ExternalInput").ap())
    args.append(nc.dram_tensor("out_0", (ITEMS, S, D), F32, kind="ExternalOutput").ap())
    graph_block_program(nc, *args)
    r = run_bass_kernel_spmd(nc, [arrays], core_ids=[0])
    return r.results[0]["out_0"]
```
